# Optimizing a Trainium2 kernel written in Bass

```python
import numpy as np
import jax
import jax.numpy as jnp

def _softmax(x, axis=-1):
    return jax.nn.softmax(x, axis=axis)

def _gelu(x):
    return jax.nn.gelu(x, approximate=True)

def _silu(x):
    return jax.nn.silu(x)

def _sigmoid(x):
    return jax.nn.sigmoid(x)

def _layernorm(x, axis=-1, eps=1e-05):
    m = jnp.mean(x, axis=axis, keepdims=True)
    v = jnp.var(x, axis=axis, keepdims=True)
    return (x - m) / jnp.sqrt(v + eps)

def _scatter_add(tgt, idx, src, axis=0):
    return tgt.at[idx].add(src)

def _segment_sum(src, seg, n):
    return jax.ops.segment_sum(src, seg, n)
kernel_name = 'mk_macaron_d2_jaxref_r8_463be0'

def setup_inputs(seed: int=0):
    np.random.seed(seed)
    _w = jnp.asarray

    def _L0_attn_setup():
        import jax, jax.numpy as jnp
        import numpy as np
        HDC_DIM = 512
        N_HEADS = 4
        HEAD_DIM = HDC_DIM // N_HEADS

        def _ste_sign(w):
            alpha = jnp.mean(jnp.abs(w), axis=-1, keepdims=True)
            hard = alpha * jnp.sign(w)
            hard = jnp.where(hard == 0, alpha, hard)
            return jax.lax.stop_gradient(hard - w) + w
        key = jax.random.key(seed)
        kx, kq, kk, kv = jax.random.split(key, 4)
        B, T = (4, 256)
        x = jax.random.normal(kx, (B, T, HDC_DIM), dtype=jnp.float32)
        bv_q = jax.random.normal(kq, (N_HEADS, HEAD_DIM), dtype=jnp.float32) * 0.02
        bv_k = jax.random.normal(kk, (N_HEADS, HEAD_DIM), dtype=jnp.float32) * 0.02
        bv_v = jax.random.normal(kv, (N_HEADS, HEAD_DIM), dtype=jnp.float32) * 0.02
        return {'x': x, 'bv_q': bv_q, 'bv_k': bv_k, 'bv_v': bv_v}
    _L0_attn_in = _L0_attn_setup()

    def _L0_ffn_setup():
        import jax, jax.numpy as jnp
        import numpy as np
        HID, BOT, RDIM, NSLOT, K, VB = (512, 64, 48, 128, 8, 32)
        TAU_LOW, TAU_HIGH, EARLY_EXIT = (0.5, 2.0, 0.05)

        def _uncertainty(h, Wu1, bu1, Wu2, bu2):
            var = jnp.var(h, axis=-1)
            log_var = jnp.log1p(var)
            norm_var = log_var / (jnp.mean(log_var) + 1e-06)
            learned = (jax.nn.gelu(h @ Wu1.T + bu1) @ Wu2.T + bu2)[..., 0]
            return jnp.clip(norm_var * 0.5 + jax.nn.sigmoid(learned) * 2.5, 0.0, 5.0)
        key = jax.random.key(seed)
        ks = jax.random.split(key, 12)
        B, S = (2, 256)
        return {'hidden_states': jax.random.normal(ks[0], (B, S, HID), dtype=jnp.float32), 'Wq': jax.random.normal(ks[1], (BOT, HID), dtype=jnp.float32) / np.sqrt(HID), 'Wr': jax.random.normal(ks[2], (RDIM, BOT), dtype=jnp.float32) / np.sqrt(BOT), 'aux_keys': jax.random.normal(ks[3], (NSLOT, BOT), dtype=jnp.float32) * 0.01, 'aux_values': jax.random.normal(ks[4], (NSLOT, HID), dtype=jnp.float32) * 0.02, 'Wvd': jax.random.normal(ks[5], (VB, HID), dtype=jnp.float32) * 0.1 / np.sqrt(HID), 'Wvu': jax.random.normal(ks[6], (HID, VB), dtype=jnp.float32) * 0.1 / np.sqrt(VB), 'Wu1': jax.random.normal(ks[7], (HID // 4, HID), dtype=jnp.float32) / np.sqrt(HID), 'bu1': jnp.zeros((HID // 4,), dtype=jnp.float32), 'Wu2': jax.random.normal(ks[8], (1, HID // 4), dtype=jnp.float32) * 0.01, 'bu2': jnp.zeros((1,), dtype=jnp.float32), 'gate_w1': jnp.float32(0.5), 'gate_bias': jnp.float32(-1.0), 'log_rel': jnp.zeros((NSLOT,), dtype=jnp.float32)}
    _L0_ffn_in = _L0_ffn_setup()

    def _L1_attn_setup():
        import jax, jax.numpy as jnp
        import numpy as np
        NEG_INF = -1e+30

        def rotary_pos_emb(x):
            B, T, H, D = x.shape
            exponents = (jnp.arange(0, D, 2)[:D // 2] // D).astype(jnp.float32)
            freqs = 1.0 / jnp.power(jnp.float32(1000.0), exponents)
            theta = jnp.arange(T, dtype=jnp.float32)[:, None] * freqs[None, :]
            cos = jnp.cos(theta)[None, :, None, :]
            sin = jnp.sin(theta)[None, :, None, :]
            xr = x.astype(jnp.float32).reshape(B, T, H, D // 2, 2)
            x0, x1 = (xr[..., 0], xr[..., 1])
            out = jnp.stack([x0 * cos - x1 * sin, x0 * sin + x1 * cos], axis=-1)
            return out.reshape(B, T, H, D).astype(x.dtype)

        def attention_fwd(x, wq, wk, wv, wo, n_heads=32):
            B, T, C = x.shape
            hd = C // n_heads
            xq = (x @ wq.T).reshape(B, T, n_heads, hd)
            xk = (x @ wk.T).reshape(B, T, n_heads, hd)
            xv = (x @ wv.T).reshape(B, T, n_heads, hd)
            xq = rotary_pos_emb(xq)
            xk = rotary_pos_emb(xk)
            scale = hd ** (-0.5)
            scores = jnp.einsum('bqhd,bkhd->bhqk', xq, xk) * scale
            causal = jnp.tril(jnp.ones((T, T), dtype=bool))
            scores = jnp.where(causal[None, None], scores, NEG_INF)
            probs = jax.nn.softmax(scores.astype(jnp.float32), axis=-1).astype(xq.dtype)
            out = jnp.einsum('bhqk,bkhd->bqhd', probs, xv).reshape(B, T, C)
            return out @ wo.T
        key = jax.random.key(seed)
        ks = jax.random.split(key, 5)
        B, T, C = (2, 256, 512)
        s = 0.02
        return {'x': jax.random.normal(ks[0], (B, T, C), jnp.float32), 'wq': jax.random.normal(ks[1], (C, C), jnp.float32) * s, 'wk': jax.random.normal(ks[2], (C, C), jnp.float32) * s, 'wv': jax.random.normal(ks[3], (C, C), jnp.float32) * s, 'wo': jax.random.normal(ks[4], (C, C), jnp.float32) * s}
    _L1_attn_in = _L1_attn_setup()

    def _L1_ffn_setup():
        import jax, jax.numpy as jnp
        import numpy as np
        H, F, E, K = (512, 800, 8, 2)
        B, S = (1, 64)
        key = jax.random.key(seed)
        k0, k1, k2, k3, k4 = jax.random.split(key, 5)
        x = jax.random.normal(k0, (B, S, H), dtype=jnp.float32)
        gate_w = jax.random.normal(k1, (E, H), dtype=jnp.float32) * 0.02
        w1 = jax.random.normal(k2, (E, F, H), dtype=jnp.float32) * 0.02
        w3 = jax.random.normal(k3, (E, F, H), dtype=jnp.float32) * 0.02
        w2 = jax.random.normal(k4, (E, H, F), dtype=jnp.float32) * 0.02
        return {'x': x, 'gate_w': gate_w, 'w1': w1, 'w2': w2, 'w3': w3}
    _L1_ffn_in = _L1_ffn_setup()
    _d = {'L0_attn_x': _L0_attn_in['x'], 'L0_attn_bv_q': _L0_attn_in['bv_q'], 'L0_attn_bv_k': _L0_attn_in['bv_k'], 'L0_attn_bv_v': _L0_attn_in['bv_v'], 'L0_ffn_Wq': _L0_ffn_in['Wq'], 'L0_ffn_Wr': _L0_ffn_in['Wr'], 'L0_ffn_aux_keys': _L0_ffn_in['aux_keys'], 'L0_ffn_aux_values': _L0_ffn_in['aux_values'], 'L0_ffn_Wvd': _L0_ffn_in['Wvd'], 'L0_ffn_Wvu': _L0_ffn_in['Wvu'], 'L0_ffn_Wu1': _L0_ffn_in['Wu1'], 'L0_ffn_bu1': _L0_ffn_in['bu1'], 'L0_ffn_Wu2': _L0_ffn_in['Wu2'], 'L0_ffn_bu2': _L0_ffn_in['bu2'], 'L0_ffn_gate_w1': _L0_ffn_in['gate_w1'], 'L0_ffn_gate_bias': _L0_ffn_in['gate_bias'], 'L0_ffn_log_rel': _L0_ffn_in['log_rel'], 'L1_attn_wq': _L1_attn_in['wq'], 'L1_attn_wk': _L1_attn_in['wk'], 'L1_attn_wv': _L1_attn_in['wv'], 'L1_attn_wo': _L1_attn_in['wo'], 'L1_ffn_gate_w': _L1_ffn_in['gate_w'], 'L1_ffn_w1': _L1_ffn_in['w1'], 'L1_ffn_w2': _L1_ffn_in['w2'], 'L1_ffn_w3': _L1_ffn_in['w3']}
    _x0 = _d['L0_attn_x']
    _d['L0_attn_x'] = jax.random.normal(jax.random.fold_in(jax.random.key(seed), 1), (1, 1024, 512), dtype=_x0.dtype)
    del _x0
    return _d

def reference(L0_attn_x, L0_attn_bv_q, L0_attn_bv_k, L0_attn_bv_v, L0_ffn_Wq, L0_ffn_Wr, L0_ffn_aux_keys, L0_ffn_aux_values, L0_ffn_Wvd, L0_ffn_Wvu, L0_ffn_Wu1, L0_ffn_bu1, L0_ffn_Wu2, L0_ffn_bu2, L0_ffn_gate_w1, L0_ffn_gate_bias, L0_ffn_log_rel, L1_attn_wq, L1_attn_wk, L1_attn_wv, L1_attn_wo, L1_ffn_gate_w, L1_ffn_w1, L1_ffn_w2, L1_ffn_w3):

    def _L0_attn_ref(x, bv_q, bv_k, bv_v):
        import jax, jax.numpy as jnp
        import numpy as np
        HDC_DIM = 512
        N_HEADS = 4
        HEAD_DIM = HDC_DIM // N_HEADS

        def _ste_sign(w):
            alpha = jnp.mean(jnp.abs(w), axis=-1, keepdims=True)
            hard = alpha * jnp.sign(w)
            hard = jnp.where(hard == 0, alpha, hard)
            return jax.lax.stop_gradient(hard - w) + w
        B, T, D = x.shape
        H, HD = (N_HEADS, HEAD_DIM)
        scale = HD ** (-0.5)
        q_bind = _ste_sign(bv_q)
        k_bind = _ste_sign(bv_k)
        v_bind = _ste_sign(bv_v)
        xh = x.reshape(B, T, H, HD)
        Q = xh * q_bind
        K = xh * k_bind
        V = xh * v_bind
        scores = jnp.einsum('bthd,bshd->bhts', Q, K) * scale
        causal = jnp.tril(jnp.ones((T, T), dtype=bool))
        attn = jnp.where(causal, jax.nn.sigmoid(scores * 4.0), 0.0)
        out = jnp.einsum('bhts,bshd->bthd', attn, V)
        return out.reshape(B, T, D)

    def _L0_ffn_ref(hidden_states, Wq, Wr, aux_keys, aux_values, Wvd, Wvu, Wu1, bu1, Wu2, bu2, gate_w1, gate_bias, log_rel):
        import jax, jax.numpy as jnp
        import numpy as np
        HID, BOT, RDIM, NSLOT, K, VB = (512, 64, 48, 128, 8, 32)
        TAU_LOW, TAU_HIGH, EARLY_EXIT = (0.5, 2.0, 0.05)

        def _uncertainty(h, Wu1, bu1, Wu2, bu2):
            var = jnp.var(h, axis=-1)
            log_var = jnp.log1p(var)
            norm_var = log_var / (jnp.mean(log_var) + 1e-06)
            learned = (jax.nn.gelu(h @ Wu1.T + bu1) @ Wu2.T + bu2)[..., 0]
            return jnp.clip(norm_var * 0.5 + jax.nn.sigmoid(learned) * 2.5, 0.0, 5.0)
        query = hidden_states @ Wq.T
        rq = query @ Wr.T
        rk = aux_keys @ Wr.T
        router_scores = jnp.einsum('bsr,nr->bsn', rq, rk) / np.sqrt(RDIM) + log_rel
        top_scores, top_idx = jax.lax.top_k(router_scores, K)
        sel_keys = aux_keys[top_idx]
        attn = jnp.einsum('bsd,bskd->bsk', query, sel_keys) / np.sqrt(BOT) + log_rel[top_idx]
        w = jax.nn.softmax(attn, axis=-1)
        sel_vals = aux_values[top_idx]
        aux_out = jnp.einsum('bsk,bskh->bsh', w, sel_vals)
        aux_out = aux_out @ Wvd.T @ Wvu.T
        u = _uncertainty(hidden_states, Wu1, bu1, Wu2, bu2)
        u_norm = jnp.clip((u - TAU_LOW) / (TAU_HIGH - TAU_LOW), 0.0, 1.0)
        gate = jax.nn.sigmoid(gate_w1 * u_norm + gate_bias)
        gate = jnp.where(gate < EARLY_EXIT, 0.0, gate)
        return hidden_states + gate[..., None] * aux_out

    def _L1_attn_ref(x, wq, wk, wv, wo):
        import jax, jax.numpy as jnp
        import numpy as np
        NEG_INF = -1e+30

        def rotary_pos_emb(x):
            B, T, H, D = x.shape
            exponents = (jnp.arange(0, D, 2)[:D // 2] // D).astype(jnp.float32)
            freqs = 1.0 / jnp.power(jnp.float32(1000.0), exponents)
            theta = jnp.arange(T, dtype=jnp.float32)[:, None] * freqs[None, :]
            cos = jnp.cos(theta)[None, :, None, :]
            sin = jnp.sin(theta)[None, :, None, :]
            xr = x.astype(jnp.float32).reshape(B, T, H, D // 2, 2)
            x0, x1 = (xr[..., 0], xr[..., 1])
            out = jnp.stack([x0 * cos - x1 * sin, x0 * sin + x1 * cos], axis=-1)
            return out.reshape(B, T, H, D).astype(x.dtype)

        def attention_fwd(x, wq, wk, wv, wo, n_heads=32):
            B, T, C = x.shape
            hd = C // n_heads
            xq = (x @ wq.T).reshape(B, T, n_heads, hd)
            xk = (x @ wk.T).reshape(B, T, n_heads, hd)
            xv = (x @ wv.T).reshape(B, T, n_heads, hd)
            xq = rotary_pos_emb(xq)
            xk = rotary_pos_emb(xk)
            scale = hd ** (-0.5)
            scores = jnp.einsum('bqhd,bkhd->bhqk', xq, xk) * scale
            causal = jnp.tril(jnp.ones((T, T), dtype=bool))
            scores = jnp.where(causal[None, None], scores, NEG_INF)
            probs = jax.nn.softmax(scores.astype(jnp.float32), axis=-1).astype(xq.dtype)
            out = jnp.einsum('bhqk,bkhd->bqhd', probs, xv).reshape(B, T, C)
            return out @ wo.T
        return attention_fwd(x, wq, wk, wv, wo)

    def _L1_ffn_ref(x, gate_w, w1, w2, w3):
        import jax, jax.numpy as jnp
        import numpy as np
        H, F, E, K = (512, 800, 8, 2)
        B, S = (1, 64)
        b, s, h = x.shape
        xt = x.reshape(-1, h)
        T = xt.shape[0]
        logits = xt @ gate_w.T
        probs = jax.nn.softmax(logits, axis=-1)
        top_vals, top_idx = jax.lax.top_k(probs, K)
        top_vals = top_vals / jnp.sum(top_vals, axis=-1, keepdims=True)
        w_full = jnp.zeros((T, E), dtype=xt.dtype).at[jnp.arange(T)[:, None], top_idx].add(top_vals)
        h1 = jnp.einsum('th,efh->tef', xt, w1)
        h3 = jnp.einsum('th,efh->tef', xt, w3)
        act = jax.nn.silu(h1) * h3
        expert_out = jnp.einsum('tef,ehf->teh', act, w2)
        y = jnp.einsum('te,teh->th', w_full, expert_out)
        return y.reshape(b, s, h)
    x = L0_attn_x
    x = x + 0.5 * _L0_ffn_ref(_layernorm(x, axis=-1), L0_ffn_Wq, L0_ffn_Wr, L0_ffn_aux_keys, L0_ffn_aux_values, L0_ffn_Wvd, L0_ffn_Wvu, L0_ffn_Wu1, L0_ffn_bu1, L0_ffn_Wu2, L0_ffn_bu2, L0_ffn_gate_w1, L0_ffn_gate_bias, L0_ffn_log_rel)
    x = x + _L0_attn_ref(_layernorm(x, axis=-1), L0_attn_bv_q, L0_attn_bv_k, L0_attn_bv_v)
    x = x + 0.5 * _L0_ffn_ref(_layernorm(x, axis=-1), L0_ffn_Wq, L0_ffn_Wr, L0_ffn_aux_keys, L0_ffn_aux_values, L0_ffn_Wvd, L0_ffn_Wvu, L0_ffn_Wu1, L0_ffn_bu1, L0_ffn_Wu2, L0_ffn_bu2, L0_ffn_gate_w1, L0_ffn_gate_bias, L0_ffn_log_rel)
    x = x + 0.5 * _L1_ffn_ref(_layernorm(x, axis=-1), L1_ffn_gate_w, L1_ffn_w1, L1_ffn_w2, L1_ffn_w3)
    x = x + _L1_attn_ref(_layernorm(x, axis=-1), L1_attn_wq, L1_attn_wk, L1_attn_wv, L1_attn_wo)
    x = x + 0.5 * _L1_ffn_ref(_layernorm(x, axis=-1), L1_ffn_gate_w, L1_ffn_w1, L1_ffn_w2, L1_ffn_w3)
    return x

_drawn_inputs = setup_inputs


def setup_inputs(seed=0):
    import zlib

    import numpy as np

    out = dict(_drawn_inputs(seed))
    spreads = {'L0_ffn_bu1': (0.0, 2.0), 'L0_ffn_log_rel': (0.0, 2.0)}
    factors = {'L0_attn_bv_q': 8.0,
     'L0_attn_bv_k': 8.0,
     'L0_ffn_Wq': 8.0,
     'L0_ffn_Wr': 8.0,
     'L0_ffn_aux_keys': 8.0,
     'L0_ffn_aux_values': 8.0,
     'L0_ffn_Wvd': 8.0,
     'L0_ffn_Wvu': 8.0,
     'L0_ffn_Wu1': 64.0,
     'L0_ffn_Wu2': 64.0,
     'L1_attn_wq': 8.0,
     'L1_attn_wk': 8.0,
     'L1_attn_wv': 5.265,
     'L1_attn_wo': 5.184,
     'L1_ffn_gate_w': 2.988}
    for name, (base, spread) in spreads.items():
        noise = np.random.default_rng([zlib.crc32(name.encode()), seed]).standard_normal(out[name].shape)
        drawn = base * np.exp(spread * noise) if base else spread * noise
        out[name] = jnp.asarray(drawn.astype(out[name].dtype))
    for name, factor in factors.items():
        out[name] = (out[name] * factor).astype(out[name].dtype)
    return out
```

```python
from contextlib import ExitStack

import numpy as np

import concourse.bass as bass
from concourse import mybir

ALU = mybir.AluOpType
ACT = mybir.ActivationFunctionType
AX = mybir.AxisListType
F32 = mybir.dt.float32
BF16 = mybir.dt.bfloat16
U32 = mybir.dt.uint32

P = 128
T, D = 1024, 512
NT = T // P
C = D // P
HT_ = T // 2
BOT, RDIM, NSLOT, VB = 64, 48, 128, 32
NH0 = 4
NH1, HD1 = 32, 16
GH = 4
NG = NH1 // GH
SLOTS = 6
KS = SLOTS * HD1
VC = HD1 + 1
NE, FF, TOPK = 8, 800, 2
NBLK = (T * TOPK + NE * (P - 1)) // P
NPAIR = [NBLK - NBLK // 2, NBLK // 2]
FH = FF // 2
FC = FF // P
FR = FF - FC * P
EPS = 1e-5
NEG = -1.0e30
HOLE = -3.0e38

PSUM_F = 512


def macaron_program(nc, A, out, stages=6):
    ctx = ExitStack()
    with ctx:
        def sb(name, shape, dt=F32):
            return ctx.enter_context(nc.sbuf_tensor(name, shape, dt))

        def sem(name):
            return ctx.enter_context(nc.semaphore(name))

        X = sb("X", [P, NT, D])
        H = sb("H", [P, NT, D])
        HT = sb("HT", [P, C, T])
        ident = sb("ident", [P, P])
        identb = sb("identb", [P, P], BF16)
        mask_ts = sb("mask_ts", [P, P], BF16)
        mask_st = sb("mask_st", [P, P], BF16)
        tri = sb("tri", [P, P])
        ones = sb("ones", [P, P])
        meanw = sb("meanw", [P, P])
        small = sb("small", [P, 64])
        blk_iota = sb("blk_iota", [1, NBLK, NE])
        STAT = sb("STAT", [P, NT, 6])
        MV = sb("MV", [P, NT, 2])
        RS = sb("RS", [P, NT])
        VE = sb("VE", [P, NT])
        MH = sb("MH", [P, NT])
        iota8, j128 = small[:, 0:8], small[:, 8:16]
        cosv, sinv = small[:, 16:24], small[:, 24:32]
        bu2, gw1, gbias, bu1 = (small[:, 32 + k:33 + k] for k in range(4))
        wqT = sb("wqT", [P, C, BOT])
        wu1T = sb("wu1T", [P, C, P])
        wu2T = sb("wu2T", [P, 1])
        LR = sb("LR", [P, NSLOT])
        MK = sb("MK", [BOT, 2 * NSLOT])
        U = sb("U", [NSLOT, D])
        QKB = sb("QKB", [P, NH0])
        VBR = sb("VBR", [P, D])
        gateT = sb("gateT", [P, C, NE])
        ARENA_F = 32896
        arena = sb("arena", [P, ARENA_F])

        def carve():
            at = [0]

            def take(shape, dt=F32, parts=P):
                n = int(np.prod(shape))
                words = n if dt in (F32, U32) else (n + 1) // 2
                ap = arena[0:parts, at[0]:at[0] + words]
                at[0] += words
                assert at[0] <= ARENA_F, at[0]
                if dt != F32:
                    ap = ap.bitcast(dt)
                if len(shape) > 1:
                    names = "abcdefg"[:len(shape)]
                    ap = ap.rearrange(f"p ({' '.join(names)}) -> p {' '.join(names)}",
                                      **{k: v for k, v in zip(names, shape)})
                return ap
            return take

        PS = ctx.enter_context(nc.psum_tensor("PS", [P, 8, PSUM_F], F32))

        s_const = sem("s_const")
        s_xin = sem("s_xin")
        stage_end = sem("stage_end")
        s_moments = sem("s_moments")
        s_rstd = sem("s_rstd")
        s_h = sem("s_h")
        s_tr = sem("s_tr")
        s_ht = sem("s_ht")
        c_dve, c_act, c_pool = sem("c_dve"), sem("c_act"), sem("c_pool")
        sems = {}

        def S(name):
            if name not in sems:
                sems[name] = sem(name)
            return sems[name]

        counts = {"dve": 0, "act": 0, "pool": 0}

        def chain(eng, key, s):
            def link(ins):
                counts[key] += 1
                ins.then_inc(s, 1)
                eng.wait_ge(s, counts[key])
                return ins
            return link

        def end_stage(eng, k, engines=4):
            eng.drain().then_inc(stage_end, 1)
            eng.wait_ge(stage_end, engines * (k + 1))

        SL = ["ffn0", "attn0", "ffn0", "moe", "attn1", "moe"][:stages]

        take = carve()
        valuesT = take([C, NSLOT])
        wvdT = take([C, VB])
        wvuT = take([D], parts=VB)
        wrT = take([RDIM], parts=BOT)
        wr = take([BOT], parts=RDIM)
        keysT = take([NSLOT], parts=BOT)
        rk = take([NSLOT], parts=RDIM)
        a1 = take([NSLOT], parts=VB)
        binds = take([3, P], parts=NH0)
        b_abs = take([3, P], parts=NH0)
        b_alpha = take([3], parts=NH0)
        b_hard = take([3, P], parts=NH0)
        b_qk = take([P], parts=NH0)
        headsel = take([NH0, P], parts=NH0)

        ZERO = arena[:, ARENA_F - D:ARENA_F]

        take = carve()
        XH = take([NT, D])
        qT = take([T], parts=BOT)
        gT = take([T])
        SCR = take([NT, NSLOT])
        ATT = take([NT, NSLOT])
        REP = take([NT, NSLOT])
        EW = take([NT, NSLOT])
        EWT = take([NT, P])
        M8 = take([NT, 8])
        NMX = take([NT])
        SM = take([NT])
        VH, LV, NORM, SGL, UN, GT, GM, RSM = (take([NT]) for _ in range(8))
        ML = take([1])

        take = carve()
        HST = take([C, T])
        AT0 = take([4, HT_])
        OV0 = take([2, HT_])

        take = carve()
        W13 = take([2, 2, C, FF])
        W2A = take([2, FC, D])
        W2B = take([2, D], parts=FR)
        XB = take([2, D])
        XBT = take([C, P])
        SG = take([2, FH])
        AC = take([FF])
        ACT_T = take([FC, P])
        ACT_R = take([P], parts=FR)
        YB = take([2, D])
        LGT = take([T], parts=NE)
        RT = sb("RT", [P, 1500])
        rt = [0]

        def rtake(shape, dt=F32, parts=P):
            n = int(np.prod(shape))
            ap = RT[0:parts, rt[0]:rt[0] + n]
            rt[0] += n
            assert rt[0] <= 1500
            if dt != F32:
                ap = ap.bitcast(dt)
            if len(shape) > 1:
                names = "abcdefg"[:len(shape)]
                ap = ap.rearrange(f"p ({' '.join(names)}) -> p {' '.join(names)}",
                                  **{k: v for k, v in zip(names, shape)})
            return ap

        LG = rtake([NT, NE])
        PR = rtake([NT, NE])
        LMX = rtake([NT])
        LSM = rtake([NT])
        V8 = rtake([NT, 8])
        I8 = rtake([NT, 8], U32)
        IF = rtake([NT, 2])
        WT = rtake([NT, 2])
        WS = rtake([NT])
        OH = rtake([NT, 2, NE])
        MM = rtake([NT, NE])
        OFF = rtake([NT + 1, NE])
        NB8 = rtake([NE, 8])
        BB = rtake([NE + 1])
        NBK = rtake([NE])
        POSE = rtake([NT, NE])
        POSK = rtake([NT, 2, NE])
        POSF = rtake([NT, 2])
        POS = rtake([NT, 2], U32)
        EBC = rtake([NBLK, NE], parts=1)
        EBF = rtake([NBLK], parts=1)
        EB = rtake([NBLK], U32, parts=1)
        take = carve()
        YG0 = take([NT, D])
        YG1 = take([NT, D])

        XG = nc.dram_tensor("xg_scratch", [NBLK * P, D], F32, kind="Internal").ap()
        YG = nc.dram_tensor("yg_scratch", [NBLK * P, D], F32, kind="Internal").ap()


        take = carve()
        WQKV = take([3, C, D])
        take = carve()
        QT = take([2, GH, T], BF16)
        KT = take([2, GH, T], BF16)
        WO = take([C, D])
        QR = take([NT, D])
        KR = take([NT, D])
        VAW = NH1 * VC + (32 - VC)
        VA = take([NT, VAW])
        QS = take([2, NT, GH, SLOTS, HD1], BF16)
        TMP = take([2, NT * GH * HD1])
        MP = take([GH, 12])
        NM2 = take([2, NT, GH])
        M3 = take([NT, GH, 3], BF16)
        PB = take([4, 2, HT_])
        OT = take([HT_])
        REC = take([4 * GH])
        OTM = H
        OTT = HT

        block = ctx.enter_context(nc.Block())

        def cols(J, i):
            return max(J * HT_, i * P), (J + 1) * HT_

        STEPS0 = [(h, J, i) for h in range(NH0) for J in range(2) for i in range(4 * J + 4)]

        SMALL_LOADS = [
            (ident, "ident"), (identb, "identb"), (mask_ts, "mask_ts"), (mask_st, "mask_st"),
            (tri, "tri"), (small, "small"), (blk_iota, "blk_iota"), (headsel, "headsel"),
            (wqT, "ffn_wqT"), (wu1T, "ffn_wu1T"), (wu2T, "ffn_wu2T"), (LR, "ffn_lr"),
            (gateT, "gateT"), (valuesT, "valuesT"), (wvdT, "wvdT"), (wvuT, "wvuT"),
            (wrT, "wrT"), (wr, "wr"), (keysT, "keysT"), (binds, "binds"),
        ]

        def sp_init(eng):
            for i in range(NT):
                eng.dma_start(X[:, i, :], A["x"][i * P:(i + 1) * P, :]).then_inc(s_xin, 16)
            for dst, name in SMALL_LOADS:
                eng.dma_start(dst if isinstance(dst, bass.AP) else dst[:], A[name]).then_inc(s_const, 16)

            eng.wait_ge(S("s_zero"), 1)
            for b in range(NBLK):
                eng.dma_start(XG[b * P:(b + 1) * P, :], ZERO).then_inc(S("s_fill"), 16)

        N_CONST = 16 * len(SMALL_LOADS)

        def dve_init(eng, link):
            eng.memset(ones[:], 1.0)
            eng.memset(meanw[:], 1.0 / T)
            eng.memset(ZERO, 0.0).then_inc(S("s_zero"), 1)
            eng.wait_ge(s_const, N_CONST)
            link(eng.scalar_tensor_tensor(b_abs, binds, -1.0, binds, ALU.mult, ALU.max))
            link(eng.tensor_reduce(b_alpha, b_abs, AX.X, ALU.add))
            link(eng.tensor_scalar(b_alpha, b_alpha, 1.0 / P, None, ALU.mult))
            link(eng.tensor_scalar(b_abs, binds, 0.0, 2.0, ALU.is_ge, ALU.mult))
            link(eng.tensor_scalar(b_abs, b_abs, 1.0, None, ALU.subtract))
            for n in range(3):
                link(eng.scalar_tensor_tensor(b_hard[:, n, :], b_abs[:, n, :], b_alpha[:, n:n + 1], binds[:, n, :],
                                              ALU.mult, ALU.subtract))
            link(eng.tensor_tensor(b_hard, b_hard, binds, ALU.add))
            eng.tensor_tensor(b_qk, b_hard[:, 0, :], b_hard[:, 1, :], ALU.mult).then_inc(S("s_binds"), 1)
            eng.tensor_copy(MK[:, NSLOT:2 * NSLOT], keysT)
            eng.wait_ge(S("s_pre1"), 2)
            eng.tensor_copy(a1, PS[0:VB, 0, 0:NSLOT])
            eng.tensor_copy(rk, PS[0:RDIM, 2, 0:NSLOT]).then_inc(S("s_pre1c"), 1)
            eng.wait_ge(S("s_pre2"), 4)
            eng.tensor_copy(U[:], PS[:, 1, :])
            eng.tensor_copy(MK[:, 0:NSLOT], PS[0:BOT, 3, 0:NSLOT])
            eng.tensor_copy(QKB[:], PS[:, 4, 0:NH0])
            link(eng.tensor_copy(VBR[:], PS[:, 5, :]))
            eng.drain().then_inc(S("s_init"), 1)

        def pe_init(eng):
            eng.wait_ge(s_const, N_CONST)
            for c in range(C):
                mm = eng.matmul(PS[0:VB, 0, 0:NSLOT], wvdT[:, c, :], valuesT[:, c, :], start=(c == 0), stop=(c == C - 1))
            mm.then_inc(S("s_pre1"), 1)
            eng.matmul(PS[0:RDIM, 2, 0:NSLOT], wrT, keysT, start=True, stop=True).then_inc(S("s_pre1"), 1)
            eng.wait_ge(S("s_pre1c"), 1)
            eng.matmul(PS[:, 1, :], a1, wvuT, start=True, stop=True).then_inc(S("s_pre2"), 1)
            eng.matmul(PS[0:BOT, 3, 0:NSLOT], wr, rk, start=True, stop=True).then_inc(S("s_pre2"), 1)
            eng.wait_ge(S("s_binds"), 1)
            eng.transpose(PS[:, 4, 0:NH0], b_qk, ident[0:NH0, 0:NH0]).then_inc(S("s_pre2"), 1)
            for h in range(NH0):
                mm = eng.matmul(PS[:, 5, h * P:(h + 1) * P], headsel[:, h, :], b_hard[:, 2, :], start=True, stop=True)
            mm.then_inc(S("s_pre2"), 1)
            eng.wait_ge(S("s_init"), 1)

        def dve_front(eng, link, k):
            if k == 0:
                eng.wait_ge(s_xin, 16 * NT)
            for J in range(2):
                for i in range(4 * J, 4 * J + 4):
                    ins = eng.bn_stats(STAT[:, i, :], X[:, i, :])
                link(ins)
                for i in range(4 * J, 4 * J + 4):
                    ins = eng.bn_aggr(MV[:, i, :], STAT[:, i, :])
                ins.then_inc(s_moments, 1)
            for J in range(2):
                eng.wait_ge(s_rstd, 2 * k + J + 1)
                for i in range(4 * J, 4 * J + 4):
                    eng.tensor_scalar(H[:, i, :], X[:, i, :], MV[:, i, 0:1], RS[:, i:i + 1],
                                      ALU.subtract, ALU.mult).then_inc(s_h, 1)

        def pool_front(eng, link, k):
            if k == 0:
                link(eng.memset(MH[:], -0.5))
            for J in range(2):
                eng.wait_ge(s_moments, 2 * k + J + 1)
                link(eng.tensor_scalar(VE[:, 4 * J:4 * J + 4], MV[:, 4 * J:4 * J + 4, 1], EPS, None, ALU.add))
                eng.tensor_tensor(RS[:, 4 * J:4 * J + 4], VE[:, 4 * J:4 * J + 4], MH[:, 4 * J:4 * J + 4],
                                  ALU.pow).then_inc(s_rstd, 1)

        def pe_front(eng, k):
            for i in range(NT):
                eng.wait_ge(s_h, NT * k + i + 1)
                if i >= 2:
                    eng.wait_ge(s_ht, NT * k + i - 1)
                for c in range(C):
                    tr = eng.transpose(PS[:, i % 2, c * P:(c + 1) * P], H[:, i, c * P:(c + 1) * P], ident[:])
                tr.then_inc(s_tr, 1)

        def act_front(eng, k):
            for i in range(NT):
                eng.wait_ge(s_tr, NT * k + i + 1)
                eng.copy(HT[:, :, i * P:(i + 1) * P],
                         PS[:, i % 2, :].rearrange("p (c t) -> p c t", c=C)).then_inc(s_ht, 1)

        def pe_ffn0(eng, k, f):
            for J in range(2):
                eng.wait_ge(s_ht, NT * k + 4 * J + 4)
                t = slice(J * HT_, (J + 1) * HT_)
                for c in range(C):
                    mm = eng.matmul(PS[0:BOT, 2 + 2 * J, :], wqT[:, c, :], HT[:, c, t], start=(c == 0), stop=(c == C - 1))
                mm.then_inc(S("s_q"), 1)
                for c in range(C):
                    mm = eng.matmul(PS[:, 3 + 2 * J, :], wu1T[:, c, :], HT[:, c, t], start=(c == 0), stop=(c == C - 1))
                mm.then_inc(S("s_u"), 1)
            for i in range(NT):
                eng.wait_ge(S("s_qc"), 2 * f + i // 4 + 1)
                if i >= 2:
                    eng.wait_ge(S("s_scc"), NT * f + i - 1)
                eng.matmul(PS[:, i % 2, 0:2 * NSLOT], qT[:, i * P:(i + 1) * P], MK[:], start=True,
                           stop=True).then_inc(S("s_sc"), 1)
            for i in range(NT):
                eng.wait_ge(S("s_g"), 2 * f + i // 4 + 1)
                mm = eng.matmul(PS[:, 6, i:i + 1], gT[:, i * P:(i + 1) * P], wu2T[:], start=True, stop=True)
            mm.then_inc(S("s_lrn"), 1)
            eng.wait_ge(S("s_lv"), f + 1)
            eng.matmul(PS[:, 7, 0:NT], meanw[:], LV, start=True, stop=True).then_inc(S("s_ml"), 1)
            for i in range(NT):
                eng.wait_ge(S("s_ew"), NT * f + i + 1)
                tr = eng.transpose(PS[:, 2 + i // 4, (i % 4) * P:(i % 4 + 1) * P], EW[:, i, :], ident[:])
                if i % 4 == 3:
                    tr.then_inc(S("s_ewt"), 1)
            for i in range(NT):
                eng.wait_ge(S("s_ewc"), 2 * f + i // 4 + 1)
                if i >= 4:
                    eng.wait_ge(S("s_x0"), NT * f + i - 3)
                if i == 0:
                    eng.wait_ge(S("s_scc"), NT * f + NT)
                eng.matmul(PS[:, (4, 5, 0, 1)[i % 4], :], EWT[:, i, :], U[:], start=True, stop=True).then_inc(S("s_aux"), 1)

        def act_ffn0(eng, link, k, f):
            for J in range(2):
                eng.wait_ge(S("s_u"), 2 * f + J + 1)
                eng.activation(gT[:, J * HT_:(J + 1) * HT_], PS[:, 3 + 2 * J, :], ACT.Gelu_apprx_tanh,
                               bias=bu1).then_inc(S("s_g"), 1)
            eng.wait_ge(S("s_vh"), f + 1)
            eng.activation(LV, VH, ACT.Ln, bias=1.0).then_inc(S("s_lv"), 1)
            eng.wait_ge(S("s_nmx"), f + 1)
            for i in range(NT):
                eng.activation(EW[:, i, :], ATT[:, i, :], ACT.Exp, bias=NMX[:, i:i + 1],
                               accum_out=SM[:, i:i + 1]).then_inc(S("s_ew"), 1)
            eng.wait_ge(S("s_lrn"), f + 1)
            eng.activation(SGL, PS[:, 6, 0:NT], ACT.Sigmoid, bias=bu2).then_inc(S("s_sgl"), 1)
            eng.wait_ge(S("s_un"), f + 1)
            eng.activation(GT, UN, ACT.Sigmoid, bias=gbias, scale=gw1).then_inc(S("s_gt"), 1)

        def dve_ffn0(eng, link, k, f):
            for i in range(NT):
                eng.wait_ge(s_h, NT * k + i + 1)
                ins = eng.bn_stats(STAT[:, i, :], H[:, i, :])
            link(ins)
            for i in range(NT):
                ins = eng.bn_aggr(MV[:, i, :], STAT[:, i, :])
            link(ins)
            eng.tensor_copy(VH, MV[:, :, 1]).then_inc(S("s_vh"), 1)
            for J in range(2):
                eng.wait_ge(S("s_q"), 2 * f + J + 1)
                eng.tensor_copy(qT[:, J * HT_:(J + 1) * HT_], PS[0:BOT, 2 + 2 * J, :]).then_inc(S("s_qc"), 1)
            for i in range(NT):
                eng.wait_ge(S("s_sc"), NT * f + i + 1)
                eng.scalar_tensor_tensor(SCR[:, i, :], PS[:, i % 2, 0:NSLOT], RDIM ** -0.5, LR[:], ALU.mult, ALU.add)
                eng.scalar_tensor_tensor(ATT[:, i, :], PS[:, i % 2, NSLOT:2 * NSLOT], BOT ** -0.5, LR[:],
                                         ALU.mult, ALU.add).then_inc(S("s_scc"), 1)
            eng.wait_ge(S("s_scc"), NT * f + NT)
            for i in range(NT):
                ins = eng.max(M8[:, i, :], SCR[:, i, :])
            link(ins)
            for i in range(NT):
                ins = eng.match_replace(REP[:, i, :], M8[:, i, :], SCR[:, i, :], HOLE)
            link(ins)
            link(eng.tensor_scalar(REP, REP, HOLE / 3, NEG, ALU.is_gt, ALU.mult))
            link(eng.tensor_tensor(ATT, ATT, REP, ALU.add))
            eng.tensor_reduce(NMX, ATT, AX.X, ALU.max, negate=True).then_inc(S("s_nmx"), 1)
            for i in range(NT):
                ins = eng.scalar_tensor_tensor(XH[:, i, :], H[:, i, :], 0.5, X[:, i, :], ALU.mult, ALU.add)
            for J in range(2):
                eng.wait_ge(S("s_ewt"), 2 * f + J + 1)
                eng.tensor_copy(EWT[:, 4 * J:4 * J + 4, :],
                                PS[:, 2 + J, :].rearrange("p (a t) -> p a t", a=4)).then_inc(S("s_ewc"), 1)
            eng.wait_ge(S("s_ml"), f + 1)
            link(eng.tensor_reduce(ML, PS[:, 7, 0:NT], AX.X, ALU.add))
            link(eng.tensor_scalar(ML, ML, 1e-6, None, ALU.add))
            link(eng.reciprocal(ML, ML))
            link(eng.tensor_scalar(NORM, LV, ML, 0.5, ALU.mult, ALU.mult))
            eng.wait_ge(S("s_sgl"), f + 1)
            link(eng.scalar_tensor_tensor(UN, SGL, 2.5, NORM, ALU.mult, ALU.add))
            link(eng.tensor_scalar(UN, UN, 0.0, 5.0, ALU.max, ALU.min))
            link(eng.tensor_scalar(UN, UN, 0.5, 1.0 / 1.5, ALU.subtract, ALU.mult))
            eng.tensor_scalar(UN, UN, 0.0, 1.0, ALU.max, ALU.min).then_inc(S("s_un"), 1)
            link(eng.reciprocal(RSM, SM))
            eng.wait_ge(S("s_gt"), f + 1)
            link(eng.scalar_tensor_tensor(GM, GT, 0.05, GT, ALU.is_ge, ALU.mult))
            link(eng.scalar_tensor_tensor(GM, GM, 0.5, RSM, ALU.mult, ALU.mult))
            for i in range(NT):
                eng.wait_ge(S("s_aux"), NT * f + i + 1)
                eng.scalar_tensor_tensor(X[:, i, :], PS[:, (4, 5, 0, 1)[i % 4], :], GM[:, i:i + 1], XH[:, i, :],
                                         ALU.mult, ALU.add).then_inc(S("s_x0"), 1)
            eng.wait_ge(S("s_x0"), NT * f + NT)

        LAG0 = 2

        def pe_attn0(eng, k):
            eng.wait_ge(s_ht, NT * k + NT)
            for n in range(len(STEPS0) + LAG0):
                if n < len(STEPS0):
                    h, J, i = STEPS0[n]
                    a, b = cols(J, i)
                    eng.wait_ge(S("s_hst"), h + 1)
                    if n >= 4:
                        eng.wait_ge(S("s_a0"), n - 3)
                    diag = i >= 4 * J
                    mm = eng.matmul(PS[:, 2 + n % 4, 0:b - a], HST[:, h, i * P:(i + 1) * P], HT[:, h, a:b],
                                    start=True, stop=not diag, skip_group_check=True)
                    if diag:
                        mm = eng.matmul(PS[:, 2 + n % 4, 0:P], identb[:], mask_st[:], start=False, stop=True,
                                        skip_group_check=True)
                    mm.then_inc(S("s_s0"), 1)
                m = n - LAG0
                if m >= 0:
                    h, J, i = STEPS0[m]
                    a, b = cols(J, i)
                    g = 2 * h + J
                    eng.wait_ge(S("s_a0"), m + 1)
                    if i == 0 and g >= 2:
                        eng.wait_ge(S("s_o0c"), g - 1)
                    for j in range(a // P, b // P):
                        jj = j - 4 * J
                        mm = eng.matmul(PS[:, 6 + g % 2, jj * P:(jj + 1) * P], AT0[:, m % 4, j * P - a:(j + 1) * P - a],
                                        H[:, i, h * P:(h + 1) * P], start=(i == 0 and jj == 0), stop=(i == j),
                                        skip_group_check=True)
                    mm.then_inc(S("s_av0"), 1)

        def act_attn0(eng, link, k):
            for n, (h, J, i) in enumerate(STEPS0):
                a, b = cols(J, i)
                eng.wait_ge(S("s_s0"), n + 1)
                if n >= 4:
                    eng.wait_ge(S("s_av0"), n - 3)
                eng.activation(AT0[:, n % 4, 0:b - a], PS[:, 2 + n % 4, 0:b - a], ACT.Sigmoid,
                               scale=4.0 * P ** -0.5).then_inc(S("s_a0"), 1)

        def dve_attn0(eng, link, k):
            eng.wait_ge(s_ht, NT * k + NT)
            for h in range(NH0):
                eng.tensor_scalar(HST[:, h, :], HT[:, h, :], QKB[:, h:h + 1], None, ALU.mult).then_inc(S("s_hst"), 1)
            done = 0
            for h in range(NH0):
                for J in range(2):
                    g = 2 * h + J
                    done += 4 * J + 4
                    eng.wait_ge(S("s_av0"), done)
                    vb = VBR[:, h * P:(h + 1) * P].unsqueeze(1).broadcast_to([P, 4, P])
                    eng.tensor_tensor(OV0[:, g % 2, :].rearrange("p (a d) -> p a d", a=4),
                                      PS[:, 6 + g % 2, :].rearrange("p (a d) -> p a d", a=4), vb,
                                      ALU.mult).then_inc(S("s_o0c"), 1)
                    eng.wait_ge(S("s_o0c"), g + 1)
                    xs = X[:, 4 * J:4 * J + 4, h * P:(h + 1) * P]
                    ins = eng.tensor_tensor(xs, xs, OV0[:, g % 2, :].rearrange("p (a d) -> p a d", a=4), ALU.add)
            link(ins)

        xg_in = [sem("xg_in0"), sem("xg_in1")]
        w13_in = [sem("w13_in0"), sem("w13_in1")]
        w2_in = [sem("w2_in0"), sem("w2_in1")]
        y_out = [sem("y_out0"), sem("y_out1")]
        NB2 = NPAIR[0]
        assert NBLK % 2 == 1

        def over_blocks(eng, body):
            for u in range(2):
                body(0, u, True, False)
            with eng.Fori(1, NB2 - 1) as n:
                for u in range(2):
                    body(n, u, False, False)
            body(NB2 - 1, 0, False, True)

        def sp_moe(eng, k, f):
            eng.wait_ge(S("s_eb"), f + 1)

            def weights(n, u, b):
                e = eng.value_load(EB[0:1, bass.ds(b, 1)], min_val=0, max_val=NE - 1)
                if not isinstance(n, int) or n >= 1:
                    eng.wait_ge(S("m_h"), 2 * (f * NBLK + b - 2) + 2)
                eng.dma_start(W13[:, u].rearrange("p m c f -> p (m c f)"),
                              A["w13"][bass.ds(e, 1)].rearrange("e p m c f -> p (e m c f)")).then_inc(w13_in[u], 16)
                if not isinstance(n, int) or n >= 1:
                    eng.wait_ge(S("m_y"), f * NBLK + b - 1)
                eng.dma_start(W2A[:, u].rearrange("p c d -> p (c d)"),
                              A["w2a"][bass.ds(e, 1)].rearrange("e p c d -> p (e c d)")).then_inc(w2_in[u], 16)
                eng.dma_start(W2B[:, u], A["w2b"][bass.ds(e, 1)].rearrange("e p d -> p (e d)")).then_inc(w2_in[u], 16)

            def rows_in(n, u, b):
                if not isinstance(n, int) or n >= 1:
                    eng.wait_ge(S("m_xtr"), f * NBLK + b - 1)
                eng.dma_start(XB[:, u], XG[bass.ds(b * P, P), :]).then_inc(xg_in[u], 16)

            weights(0, 0, 0)
            eng.wait_ge(S("s_scat"), 16 * TOPK * NT * (f + 1))
            rows_in(0, 0, 0)
            rows_in(0, 1, 1)
            weights(0, 1, 1)
            with eng.Fori(1, NB2 - 1) as n:
                for u in range(2):
                    rows_in(n, u, 2 * n + u)
                    weights(n, u, 2 * n + u)
            rows_in(NB2 - 1, 0, NBLK - 1)
            weights(NB2 - 1, 0, NBLK - 1)

        def pool_moe(eng, link, k, f):
            eng.wait_ge(S("s_pos"), f + 1)
            if f == 0:
                eng.wait_ge(S("s_fill"), 16 * NBLK)
            for i in range(NT):
                for j in range(TOPK):
                    eng.indirect_dma_start(XG[:, :], bass.IndirectOffsetOnAxis(ap=POS[:, i, j:j + 1], axis=0),
                                           H[:, i, :], None).then_inc(S("s_scat"), 16)
            for u in range(2):
                eng.wait_ge(y_out[u], 16 * NPAIR[u] * (f + 1))
            for i in range(NT):
                for j, dst in ((0, YG0), (1, YG1)):
                    eng.indirect_dma_start(dst[:, i, :], None, YG[:, :],
                                           bass.IndirectOffsetOnAxis(ap=POS[:, i, j:j + 1], axis=0)).then_inc(yg_in[i], 16)

        yg_in = [sem(f"yg_in{i}") for i in range(NT)]

        def pe_moe(eng, k, f):
            for J in range(2):
                eng.wait_ge(s_ht, NT * k + 4 * J + 4)
                for c in range(C):
                    mm = eng.matmul(PS[0:NE, 2 + J, :], gateT[:, c, :], HT[:, c, J * HT_:(J + 1) * HT_],
                                    start=(c == 0), stop=(c == C - 1))
                mm.then_inc(S("s_lgt"), 1)
            eng.wait_ge(S("s_lgtc"), 2 * f + 2)
            for i in range(NT):
                tr = eng.transpose(PS[:, 4, i * NE:(i + 1) * NE], LGT[:, i * P:(i + 1) * P], ident[0:NE, 0:NE])
            tr.then_inc(S("s_lg"), 1)
            eng.wait_ge(S("s_mm"), f + 1)
            mmv = MM.rearrange("p a b -> p (a b)")
            eng.matmul(PS[:, 5, 0:NT * NE], tri[:], mmv, start=True, stop=True)
            eng.matmul(PS[:, 6, 0:NT * NE], ones[:], mmv, start=True, stop=True).then_inc(S("s_rank"), 1)
            eng.wait_ge(S("s_pos"), f + 1)

            def turn_rows(n, u):
                eng.wait_ge(xg_in[u], 16 * (NPAIR[u] * f + n + 1))
                for c in range(C):
                    tr = eng.transpose(PS[:, 6, c * P:(c + 1) * P], XB[:, u, c * P:(c + 1) * P], ident[:])
                tr.then_inc(S("m_xtr"), 1)

            def hidden(B, u, hf, chunks, first):
                if chunks[0] == 0 and not first:
                    eng.wait_ge(S("m_act"), 2 * B + hf - 1)
                for c in chunks:
                    for m in range(2):
                        mm = eng.matmul(PS[:, 2 * hf + m, 0:FH], XBT[:, c, :], W13[:, u, m, c, hf * FH:(hf + 1) * FH],
                                        start=(c == 0), stop=(c == C - 1))
                if chunks[-1] == C - 1:
                    mm.then_inc(S("m_h"), 1)

            def body(n, u, first, last):
                B = f * NBLK + 2 * n + u
                none_before = first and u == 0
                eng.wait_ge(S("m_xt"), B + 1)
                eng.wait_ge(w13_in[u], 16 * (NPAIR[u] * f + n + 1))
                hidden(B, u, 0, [0, 1, 2, 3], none_before)
                hidden(B, u, 1, [0, 1], none_before)
                eng.wait_ge(S("m_act"), 2 * B + 1)
                for c in range(3):
                    tr = eng.transpose(PS[:, 4, c * P:(c + 1) * P], AC[:, c * P:(c + 1) * P], ident[:])
                tr.then_inc(S("m_t0"), 1)
                hidden(B, u, 1, [2, 3], none_before)
                eng.wait_ge(w2_in[u], 32 * (NPAIR[u] * f + n + 1))
                if not none_before:
                    eng.wait_ge(S("m_yc"), B)
                eng.wait_ge(S("m_t0c"), B + 1)
                for c in range(3):
                    eng.matmul(PS[:, 7, :], ACT_T[:, c, :], W2A[:, u, c, :], start=(c == 0), stop=False)
                eng.wait_ge(S("m_act"), 2 * B + 2)
                for c in range(3, FC):
                    eng.transpose(PS[:, 5, (c - 3) * P:(c - 2) * P], AC[:, c * P:(c + 1) * P], ident[:])
                eng.transpose(PS[0:FR, 5, 3 * P:4 * P], AC[:, FC * P:FF], ident[:]).then_inc(S("m_t1"), 1)
                if not last:
                    turn_rows(n + u, 1 - u)
                eng.wait_ge(S("m_t1c"), B + 1)
                for c in range(3, FC):
                    eng.matmul(PS[:, 7, :], ACT_T[:, c, :], W2A[:, u, c, :], start=False, stop=False)
                eng.matmul(PS[:, 7, :], ACT_R, W2B[:, u, :], start=False, stop=True).then_inc(S("m_y"), 1)

            turn_rows(0, 0)
            over_blocks(eng, body)

        def act_moe(eng, link, k, f):
            eng.wait_ge(S("s_lmx"), f + 1)
            eng.activation(PR, LG, ACT.Exp).then_inc(S("s_pr"), 1)

            def rows_out(B):
                eng.wait_ge(S("m_xtr"), B + 1)
                eng.copy(XBT, PS[:, 6, :].rearrange("p (c t) -> p c t", c=C)).then_inc(S("m_xt"), 1)

            def body(n, u, first, last):
                B = f * NBLK + 2 * n + u
                for hf in range(2):
                    eng.wait_ge(S("m_h"), 2 * B + hf + 1)
                    eng.activation(SG[:, hf, :], PS[:, 2 * hf, 0:FH], ACT.Silu).then_inc(S("m_sg"), 1)
                eng.wait_ge(S("m_t1"), B + 1)
                eng.copy(ACT_T[:, 3:FC, :], PS[:, 5, 0:3 * P].rearrange("p (c t) -> p c t", c=3))
                eng.copy(ACT_R, PS[0:FR, 5, 3 * P:4 * P]).then_inc(S("m_t1c"), 1)
                if not last:
                    rows_out(B + 1)
                eng.wait_ge(S("m_y"), B + 1)
                if not (first and f == 0):
                    eng.wait_ge(y_out[u], 16 * (NPAIR[u] * f + n))
                eng.copy(YB[:, u, :], PS[:, 7, :]).then_inc(S("m_yc"), 1)
                eng.wait_ge(S("m_yc"), B + 1)
                eng.dma_start(YG[bass.ds((2 * n + u) * P, P), :], YB[:, u, :]).then_inc(y_out[u], 16)

            rows_out(f * NBLK)
            over_blocks(eng, body)

        def dve_moe(eng, link, k, f):
            for J in range(2):
                eng.wait_ge(S("s_lgt"), 2 * f + J + 1)
                eng.tensor_copy(LGT[:, J * HT_:(J + 1) * HT_], PS[0:NE, 2 + J, :]).then_inc(S("s_lgtc"), 1)
            eng.wait_ge(S("s_lg"), f + 1)
            lg = PS[:, 4, 0:NT * NE].rearrange("p (a b) -> p a b", a=NT)
            link(eng.tensor_reduce(LMX, lg, AX.X, ALU.max))
            eng.tensor_tensor(LG, lg, LMX.unsqueeze(2).broadcast_to([P, NT, NE]), ALU.subtract).then_inc(S("s_lmx"), 1)
            eng.wait_ge(S("s_pr"), f + 1)
            link(eng.tensor_reduce(LSM, PR, AX.X, ALU.add))
            link(eng.reciprocal(LSM, LSM))
            link(eng.tensor_tensor(PR, PR, LSM.unsqueeze(2).broadcast_to([P, NT, NE]), ALU.mult))
            for i in range(NT):
                ins = eng.max(V8[:, i, :], PR[:, i, :])
            link(ins)
            for i in range(NT):
                ins = eng.max_index(I8[:, i, :], V8[:, i, :], PR[:, i, :])
            link(eng.tensor_tensor(WS, V8[:, :, 0], V8[:, :, 1], ALU.add))
            link(eng.reciprocal(WS, WS))
            link(eng.tensor_tensor(WT, V8[:, :, 0:TOPK], WS.unsqueeze(2).broadcast_to([P, NT, TOPK]), ALU.mult))
            link(eng.tensor_scalar(WT, WT, 0.5, None, ALU.mult))
            link(eng.tensor_copy(IF, I8[:, :, 0:TOPK]))
            four = [P, NT, TOPK, NE]
            link(eng.tensor_tensor(OH, iota8.unsqueeze(1).unsqueeze(1).broadcast_to(four),
                                   IF.unsqueeze(3).broadcast_to(four), ALU.is_equal))
            eng.tensor_tensor(MM, OH[:, :, 0, :], OH[:, :, 1, :], ALU.add).then_inc(S("s_mm"), 1)
            link(eng.memset(OFF[:, 0, :], 0.0))
            link(eng.memset(BB[:, 0:1], 0.0))
            eng.wait_ge(S("s_rank"), f + 1)
            for i in range(NT):
                link(eng.tensor_tensor(OFF[:, i + 1, :], OFF[:, i, :], PS[:, 6, i * NE:(i + 1) * NE], ALU.add))
            eight = [P, NE, 8]
            link(eng.tensor_tensor(NB8, OFF[:, NT, :].unsqueeze(2).broadcast_to(eight),
                                   j128.unsqueeze(1).broadcast_to(eight), ALU.is_gt))
            link(eng.tensor_reduce(NBK, NB8, AX.X, ALU.add))
            for e in range(NE):
                link(eng.tensor_tensor(BB[:, e + 1:e + 2], BB[:, e:e + 1], NBK[:, e:e + 1], ALU.add))
            link(eng.tensor_scalar(NBK, BB[:, 0:NE], float(P), None, ALU.mult))
            link(eng.tensor_tensor(POSE, PS[:, 5, 0:NT * NE].rearrange("p (a b) -> p a b", a=NT), OFF[:, 0:NT, :], ALU.add))
            link(eng.tensor_tensor(POSE, POSE, NBK.unsqueeze(1).broadcast_to([P, NT, NE]), ALU.add))
            link(eng.tensor_tensor(POSK, OH, POSE.unsqueeze(2).broadcast_to(four), ALU.mult))
            link(eng.tensor_reduce(POSF, POSK, AX.X, ALU.add))
            eng.tensor_copy(POS, POSF).then_inc(S("s_pos"), 1)
            ebs = [1, NBLK, NE]
            link(eng.tensor_tensor(EBC, blk_iota[:], BB[0:1, 1:NE + 1].unsqueeze(1).broadcast_to(ebs), ALU.is_ge))
            link(eng.tensor_reduce(EBF, EBC, AX.X, ALU.add))
            link(eng.tensor_scalar(EBF, EBF, NE - 1.0, None, ALU.min))
            eng.tensor_copy(EB, EBF).then_inc(S("s_eb"), 1)

            def body(n, u, first, last):
                B = f * NBLK + 2 * n + u
                for hf in range(2):
                    eng.wait_ge(S("m_sg"), 2 * B + hf + 1)
                    eng.tensor_tensor(AC[:, hf * FH:(hf + 1) * FH], SG[:, hf, :], PS[:, 2 * hf + 1, 0:FH],
                                      ALU.mult).then_inc(S("m_act"), 1)
                    if hf == 0:
                        eng.wait_ge(S("m_t0"), B + 1)
                        eng.tensor_copy(ACT_T[:, 0:3, :],
                                        PS[:, 4, 0:3 * P].rearrange("p (c t) -> p c t", c=3)).then_inc(S("m_t0c"), 1)

            over_blocks(eng, body)
            for i in range(NT):
                eng.wait_ge(yg_in[i], 16 * TOPK * (f + 1))
                link(eng.scalar_tensor_tensor(X[:, i, :], YG0[:, i, :], WT[:, i, 0:1], X[:, i, :], ALU.mult, ALU.add))
                ins = eng.scalar_tensor_tensor(X[:, i, :], YG1[:, i, :], WT[:, i, 1:2], X[:, i, :], ALU.mult, ALU.add)
            link(ins)

        QSLOT = (0, 0, 1, 1, 0, 2)
        KSLOT = (0, 1, 0, 1, 2, 0)
        SCALE1 = HD1 ** -0.5

        def plan_attn1():
            def prepare(g):
                units = [("tr", g, 0, 0), ("tr", g, 1, 0), ("tr", g, 0, 1), ("tr", g, 1, 1)]
                for h in range(GH):
                    mine = [("max", g, h, i, part) for i in range(NT) for part in range(1 if i < 4 else 2)]
                    if h + 2 < GH:
                        mine.insert(3, ("tr", g, 0, h + 2))
                        mine.insert(8, ("tr", g, 1, h + 2))
                        if h + 2 == GH - 1 and g + 1 < NG:
                            mine.insert(9, ("split", g + 1))
                    units += mine
                units.append(("shift", g))
                return units

            def between(g, n_early):
                units = prepare(g)
                early = [[u] for u in units[:n_early]]
                rest = units[n_early:]
                room = 21 - n_early
                cut = [len(rest) * m // room for m in range(room + 1)]
                tail = [[("mrow", g, h)] for h in range(GH)]
                return early + [rest[x:y] for x, y in zip(cut, cut[1:])] + [[]] + [tail[0] + tail[1]] + [tail[2] + tail[3]]

            plan = [("split", 0)] + prepare(0) + [("mrow", 0, h) for h in range(GH)]
            for g in range(NG):
                steps = [(J, i) for J in range(2) for i in range(4 * J + 4)]
                nxt = between(g + 1, 4) if g + 1 < NG else [[]] * 24
                last = None
                for n, (J, i) in enumerate(steps):
                    for pair in range(2):
                        plan.append(("exp", g, J, i, pair))
                        plan += nxt[2 * n + pair]
                    if last:
                        plan.append(("av", g) + last)
                        if last == (0, 3):
                            plan.append(("ocopy", g, 0))
                    if n == 5:
                        plan.append(("turn", g, 0))
                    last = (J, i)
                plan.append(("av", g) + last)
                plan.append(("ocopy", g, 1))
                plan.append(("turn", g, 1))
            return plan

        PLAN1 = plan_attn1()

        def widths(i, part):
            return (0, (i + 1) * P) if i < 4 else ((0, HT_) if part == 0 else (HT_, (i + 1) * P))

        def numbered():
            seen = {}
            turns = 0
            for unit in PLAN1:
                kind = unit[0]
                n = seen.get(kind, 0)
                seen[kind] = n + 1
                yield unit, n, turns
                if kind in ("tr", "mrow", "turn"):
                    turns += 1

        T2B = PS[:, 2, :].bitcast(BF16)

        def sp_attn1(eng, k):
            eng.wait_ge(stage_end, 4 * k)
            for n in range(3):
                eng.dma_start(WQKV[:, n], A["wqkv"][:, n]).then_inc(S("s_wqkv"), 16)
            eng.dma_start(WO, A["wo"]).then_inc(S("s_wo"), 16)

        def pool_attn1(eng, link, k):
            eng.memset(VA, 1.0).then_inc(S("s_va1"), 1)
            for (kind, *a), n, _ in numbered():
                if kind == "split":
                    for x, slots in ((0, QSLOT), (1, KSLOT)):
                        eng.wait_ge(S("s_split"), 2 * n + x + 1)
                        for s in range(SLOTS):
                            if slots.index(slots[s]) != s:
                                ins = eng.tensor_copy(QS[:, x, :, :, s, :], QS[:, x, :, :, slots.index(slots[s]), :])
                        ins.then_inc(S("s_dup"), 1)

        def pe_attn1(eng, k):
            eng.wait_ge(S("s_wqkv"), 48)
            for i in range(NT):
                eng.wait_ge(s_ht, NT * k + i + 1)
                if i >= 2:
                    eng.wait_ge(S("s_rot"), 2 * (i - 1))
                    eng.wait_ge(S("s_vc"), i - 1)
                for n in range(3):
                    for c in range(C):
                        mm = eng.matmul(PS[:, 2 + 3 * (i % 2) + n, :], HT[:, c, i * P:(i + 1) * P], WQKV[:, n, c, :],
                                        start=(c == 0), stop=(c == C - 1))
                    mm.then_inc(S("s_proj"), 1)
            eng.wait_ge(S("s_rot"), 2 * NT)
            eng.wait_ge(S("s_vc"), NT)
            eng.wait_ge(S("s_kones"), 1)
            for (kind, *a), n, turns in numbered():
                if kind in ("tr", "mrow", "turn") and turns > 0:
                    eng.wait_ge(S("s_t2c"), turns)
                if kind == "tr":
                    g, x, h = a
                    eng.wait_ge(S("s_dup"), 2 * g + x + 1)
                    for i in range(NT):
                        tr = eng.transpose(T2B[0:KS, i * P:(i + 1) * P],
                                           QS[:, x, i, h].rearrange("p s d -> p (s d)"), identb[:])
                    tr.then_inc(S("s_t2"), 1)
                elif kind == "max":
                    g, h, i, part = a
                    lo, hi = widths(i, part)
                    eng.wait_ge(S("s_t2k"), GH * g + h + 1)
                    eng.wait_ge(S("s_t2q"), GH * g + h + 1)
                    if n >= 2:
                        eng.wait_ge(S("s_mx"), n - 1)
                    diag = hi == (i + 1) * P
                    mm = eng.matmul(PS[:, n % 2, 0:hi - lo], QT[0:KS, g % 2, h, i * P:(i + 1) * P], KT[0:KS, g % 2, h, lo:hi],
                                    start=True, stop=not diag, skip_group_check=True)
                    if diag:
                        mm = eng.matmul(PS[:, n % 2, hi - lo - P:hi - lo], identb[:], mask_ts[:], start=False, stop=True,
                                        skip_group_check=True)
                    mm.then_inc(S("s_sa"), 1)
                elif kind == "mrow":
                    g, h = a
                    eng.wait_ge(S("s_m3"), g + 1)
                    for i in range(NT):
                        tr = eng.transpose(T2B[KS:KS + 3, i * P:(i + 1) * P], M3[:, i, h, :], identb[:])
                    tr.then_inc(S("s_t2"), 1)
                elif kind == "exp":
                    g, J, i, pair = a
                    lo, hi = cols(J, i)
                    eng.wait_ge(S("s_mrow"), GH * g + 2 * pair + 2)
                    if n >= 2:
                        eng.wait_ge(S("s_p"), n - 1)
                    for e in range(2):
                        h = 2 * pair + e
                        bank = PS[:, 4 + 2 * (n % 2) + e, :]
                        diag = i >= 4 * J
                        mm = eng.matmul(bank[:, 0:hi - lo], KT[0:KS + 3, g % 2, h, i * P:(i + 1) * P],
                                        QT[0:KS + 3, g % 2, h, lo:hi], start=True, stop=not diag, skip_group_check=True)
                        if diag:
                            mm = eng.matmul(bank[:, 0:P], identb[:], mask_st[:], start=False, stop=True,
                                            skip_group_check=True)
                    mm.then_inc(S("s_st"), 1)
                elif kind == "av":
                    g, J, i = a
                    lo, hi = cols(J, i)
                    eng.wait_ge(S("s_p"), 2 * n + 2)
                    if i == 0 and 2 * g + J > 0:
                        eng.wait_ge(S("s_oc"), 2 * g + J)
                    for h in range(GH):
                        mm = eng.matmul(PS[32 * h:32 * h + 32, 3, lo - J * HT_:HT_],
                                        VA[:, i, (GH * g + h) * VC:(GH * g + h) * VC + 32],
                                        PB[:, (2 * n + h // 2) % 4, h % 2, 0:hi - lo],
                                        start=(i == 0), stop=(i == 4 * J + 3), skip_group_check=True)
                    mm.then_inc(S("s_av"), 1)
                elif kind == "turn":
                    g, J = a
                    eng.wait_ge(S("s_oc"), 2 * g + J + 1)
                    for j in range(4):
                        tr = eng.transpose(PS[:, 2, j * P:(j + 1) * P], OT[:, j * P:(j + 1) * P], ident[:])
                    tr.then_inc(S("s_t2"), 1)
            eng.wait_ge(S("s_wo"), 16)
            eng.wait_ge(S("s_otm"), 2 * NG)
            for i in range(NT + 1):
                if i < NT:
                    if i >= 2:
                        eng.wait_ge(S("s_ott"), i - 1)
                    for c in range(C):
                        tr = eng.transpose(PS[:, i % 2, c * P:(c + 1) * P], OTM[:, i, c * P:(c + 1) * P], ident[:])
                    tr.then_inc(S("s_ottr"), 1)
                if i >= 1:
                    j = i - 1
                    eng.wait_ge(S("s_ott"), j + 1)
                    if j >= 4:
                        eng.wait_ge(S("s_x1"), j - 3)
                    for c in range(C):
                        mm = eng.matmul(PS[:, 4 + j % 4, :], OTT[:, c, j * P:(j + 1) * P], WO[:, c, :],
                                        start=(c == 0), stop=(c == C - 1))
                    mm.then_inc(S("s_wop"), 1)

        def act_attn1(eng, link, k):
            eng.wait_ge(S("s_va1"), 1)
            for i in range(NT):
                eng.wait_ge(S("s_proj"), 3 * i + 3)
                eng.copy(VA[:, i, 0:NH1 * VC].rearrange("p (h c) -> p h c", c=VC)[:, :, 0:HD1],
                         PS[:, 4 + 3 * (i % 2), :].rearrange("p (h d) -> p h d", d=HD1)).then_inc(S("s_vc"), 1)
            eng.wait_ge(S("s_rot"), 2 * NT)
            for (kind, *a), n, turns in numbered():
                if kind == "tr" and a[1] == 1:
                    g, x, h = a
                    eng.wait_ge(S("s_t2"), turns + 1)
                    eng.copy(KT[0:KS, g % 2, h, :], T2B[0:KS, :]).then_inc(S("s_t2k"), 1)
                    eng.wait_ge(S("s_t2k"), GH * g + h + 1)
                    eng.sem_inc(S("s_t2c"), 1)
                elif kind == "mrow":
                    g, h = a
                    eng.wait_ge(S("s_t2"), turns + 1)
                    eng.copy(QT[KS:KS + 3, g % 2, h, :], T2B[KS:KS + 3, :]).then_inc(S("s_mrow"), 1)
                    eng.wait_ge(S("s_mrow"), n + 1)
                    eng.sem_inc(S("s_t2c"), 1)
                elif kind == "exp":
                    g, J, i, pair = a
                    lo, hi = cols(J, i)
                    eng.wait_ge(S("s_st"), n + 1)
                    if n >= 4:
                        eng.wait_ge(S("s_av"), n // 2 - 1)
                    b = 4 + 2 * (n % 2)
                    eng.activation(PB[:, n % 4, :, 0:hi - lo], PS[:, b:b + 2, 0:hi - lo], ACT.Exp,
                                   scale=SCALE1).then_inc(S("s_p"), 1)
            for i in range(NT):
                eng.wait_ge(S("s_ottr"), i + 1)
                eng.copy(OTT[:, :, i * P:(i + 1) * P],
                         PS[:, i % 2, :].rearrange("p (c t) -> p c t", c=C)).then_inc(S("s_ott"), 1)

        def dve_attn1(eng, link, k):
            for i in range(NT):
                for n, dst in ((0, QR), (1, KR)):
                    eng.wait_ge(S("s_proj"), 3 * i + n + 1)
                    src = PS[:, 2 + 3 * (i % 2) + n, :].rearrange("p (f two) -> p f two", two=2)
                    d = dst[:, i, :].rearrange("p (f two) -> p f two", two=2)
                    t = TMP[:, n, :].rearrange("p (two f) -> p two f", two=2)
                    eng.tensor_scalar(t[:, 0], src[:, :, 1], sinv[:, i:i + 1], None, ALU.mult)
                    link(eng.tensor_scalar(t[:, 1], src[:, :, 1], cosv[:, i:i + 1], None, ALU.mult))
                    eng.scalar_tensor_tensor(d[:, :, 0], src[:, :, 0], cosv[:, i:i + 1], t[:, 0], ALU.mult, ALU.subtract)
                    eng.scalar_tensor_tensor(d[:, :, 1], src[:, :, 0], sinv[:, i:i + 1], t[:, 1],
                                             ALU.mult, ALU.add).then_inc(S("s_rot"), 1)
            eng.wait_ge(S("s_rot"), 2 * NT)
            eng.wait_ge(S("s_proj"), 3 * NT)
            eng.memset(KT[KS:KS + 3], 1.0).then_inc(S("s_kones"), 1)
            for (kind, *a), n, turns in numbered():
                if kind == "split":
                    g, = a
                    if g >= 1:
                        eng.wait_ge(S("s_t2q"), GH * g)
                        eng.wait_ge(S("s_t2k"), GH * g)
                    for x, src, slots in ((0, QR, QSLOT), (1, KR, KSLOT)):
                        v = src[:, :, g * GH * HD1:(g + 1) * GH * HD1].rearrange("p a (h d) -> p a h d", h=GH)
                        p1, p2, p3 = (QS[:, x, :, :, slots.index(m), :] for m in range(3))
                        r = TMP[:, x, :].rearrange("p (a h d) -> p a h d", a=NT, h=GH)
                        link(eng.tensor_copy(p1, v))
                        link(eng.tensor_tensor(r, v, p1, ALU.subtract))
                        link(eng.tensor_copy(p2, r))
                        eng.tensor_tensor(p3, r, p2, ALU.subtract).then_inc(S("s_split"), 1)
                elif kind == "tr" and a[1] == 0:
                    g, x, h = a
                    eng.wait_ge(S("s_t2"), turns + 1)
                    eng.tensor_copy(QT[0:KS, g % 2, h, :], T2B[0:KS, :]).then_inc(S("s_t2q"), 1)
                    eng.wait_ge(S("s_t2q"), GH * g + h + 1)
                    eng.sem_inc(S("s_t2c"), 1)
                elif kind == "max":
                    g, h, i, part = a
                    lo, hi = widths(i, part)
                    at = i if i < 4 else 4 + 2 * (i - 4) + part
                    eng.wait_ge(S("s_sa"), n + 1)
                    eng.tensor_reduce(MP[:, h, at:at + 1], PS[:, n % 2, 0:hi - lo], AX.X, ALU.max).then_inc(S("s_mx"), 1)
                elif kind == "shift":
                    g, = a
                    if g >= 1:
                        eng.wait_ge(S("s_mrow"), GH * g)
                    eng.wait_ge(S("s_mx"), 12 * GH * (g + 1))
                    mpv = MP.rearrange("p h a -> p a h")
                    late = mpv[:, 4:12, :].rearrange("p (i two) h -> p i two h", two=2)
                    eng.tensor_scalar(NM2[:, 0, 0:4, :], mpv[:, 0:4, :], -1.0, None, ALU.mult)
                    link(eng.scalar_tensor_tensor(NM2[:, 1, 4:8, :], late[:, :, 0, :], 1.0, late[:, :, 1, :], ALU.mult, ALU.max))
                    link(eng.tensor_scalar(NM2[:, 0, 4:8, :], NM2[:, 1, 4:8, :], -1.0, None, ALU.mult))
                    link(eng.tensor_copy(M3[:, :, :, 0], NM2[:, 0]))
                    link(eng.tensor_tensor(NM2[:, 1], NM2[:, 0], M3[:, :, :, 0], ALU.subtract))
                    link(eng.tensor_copy(M3[:, :, :, 1], NM2[:, 1]))
                    eng.tensor_tensor(M3[:, :, :, 2], NM2[:, 1], M3[:, :, :, 1], ALU.subtract).then_inc(S("s_m3"), 1)
                elif kind == "ocopy":
                    g, J = a
                    eng.wait_ge(S("s_av"), 12 * g + (4 if J == 0 else 12))
                    eng.tensor_copy(OT, PS[:, 3, :]).then_inc(S("s_oc"), 1)
                elif kind == "turn":
                    g, J = a
                    eng.wait_ge(S("s_t2"), turns + 1)
                    o = PS[:, 2, :].rearrange("p (a h c) -> p a h c", a=4, h=GH)
                    rec = REC.rearrange("p (a h) -> p a h", a=4)
                    link(eng.reciprocal(rec, o[:, :, :, HD1]))
                    eng.tensor_tensor(OTM[:, 4 * J:4 * J + 4, g * GH * HD1:(g + 1) * GH * HD1].rearrange(
                        "p a (h d) -> p a h d", h=GH), o[:, :, :, 0:HD1],
                        rec.unsqueeze(3).broadcast_to([P, 4, GH, HD1]), ALU.mult).then_inc(S("s_otm"), 1)
                    eng.wait_ge(S("s_otm"), n + 1)
                    eng.sem_inc(S("s_t2c"), 1)
            for i in range(NT):
                eng.wait_ge(S("s_wop"), i + 1)
                eng.tensor_tensor(X[:, i, :], X[:, i, :], PS[:, 4 + i % 4, :], ALU.add).then_inc(S("s_x1"), 1)
            eng.wait_ge(S("s_x1"), NT)

        def instance(k):
            return SL[:k].count(SL[k])

        @block.sync
        def _(sp):
            sp_init(sp)
            for k, kind in enumerate(SL):
                if kind == "moe":
                    sp_moe(sp, k, instance(k))
                if kind == "attn1":
                    sp_attn1(sp, k)
            sp.wait_ge(stage_end, 4 * len(SL))
            for i in range(NT):
                sp.dma_start(out[i * P:(i + 1) * P, :], X[:, i, :]).then_inc(S("s_out"), 16)
            sp.wait_ge(S("s_out"), 16 * NT)

        @block.gpsimd
        def _(pool):
            link = chain(pool, "pool", c_pool)
            for k, kind in enumerate(SL):
                pool_front(pool, link, k)
                if kind == "moe":
                    pool_moe(pool, link, k, instance(k))
                if kind == "attn1":
                    pool_attn1(pool, link, k)
                end_stage(pool, k)

        @block.scalar
        def _(act):
            link = chain(act, "act", c_act)
            act.wait_ge(s_const, N_CONST)
            act.wait_ge(S("s_init"), 1)
            for k, kind in enumerate(SL):
                act_front(act, k)
                if kind == "ffn0":
                    act_ffn0(act, link, k, instance(k))
                elif kind == "attn0":
                    act_attn0(act, link, k)
                elif kind == "moe":
                    act_moe(act, link, k, instance(k))
                else:
                    act_attn1(act, link, k)
                end_stage(act, k)

        @block.vector
        def _(dve):
            link = chain(dve, "dve", c_dve)
            dve_init(dve, link)
            for k, kind in enumerate(SL):
                dve_front(dve, link, k)
                if kind == "ffn0":
                    dve_ffn0(dve, link, k, instance(k))
                elif kind == "attn0":
                    dve_attn0(dve, link, k)
                elif kind == "moe":
                    dve_moe(dve, link, k, instance(k))
                else:
                    dve_attn1(dve, link, k)
                end_stage(dve, k)

        @block.tensor
        def _(pe):
            pe_init(pe)
            for k, kind in enumerate(SL):
                pe_front(pe, k)
                if kind == "ffn0":
                    pe_ffn0(pe, k, instance(k))
                elif kind == "attn0":
                    pe_attn0(pe, k)
                elif kind == "moe":
                    pe_moe(pe, k, instance(k))
                else:
                    pe_attn1(pe, k)
                end_stage(pe, k)


def laid_out(x):
    f32 = np.float32
    c = np.ascontiguousarray
    bf = mybir.dt.np(BF16)

    def rows(w):
        return c(w.reshape(-1, P, w.shape[-1]).transpose(1, 0, 2))

    p, j = np.arange(P)[:, None], np.arange(P)[None, :]
    tok = (np.arange(NT)[None, :] * P + np.arange(P)[:, None]).astype(np.float64)
    small = np.zeros((P, 64), f32)
    small[:, 0:8] = np.arange(8)
    small[:, 8:16] = P * np.arange(8)
    small[:, 16:24] = np.cos(tok)
    small[:, 24:32] = np.sin(tok)
    small[:, 32] = x["L0_ffn_bu2"].reshape(-1)
    small[:, 33] = x["L0_ffn_gate_w1"].reshape(-1)
    small[:, 34] = x["L0_ffn_gate_bias"].reshape(-1)
    small[:, 35] = x["L0_ffn_bu1"]
    w13 = np.stack([x["L1_ffn_w1"], x["L1_ffn_w3"]], 1)
    w13 = w13.transpose(0, 3, 1, 2).reshape(NE, C, P, 2, FF)
    w2 = x["L1_ffn_w2"].transpose(0, 2, 1)
    wqkv = np.stack([x[f"L1_attn_w{n}"].T.reshape(C, P, D) for n in "qkv"], 0)
    return {
        "x": c(x["L0_attn_x"].reshape(T, D)),
        "ident": np.eye(P, dtype=f32), "identb": np.eye(P, dtype=f32).astype(bf),
        "mask_ts": np.where(j > p, NEG, 0.0).astype(bf), "mask_st": np.where(p > j, NEG, 0.0).astype(bf),
        "tri": (p < j).astype(f32), "small": small,
        "blk_iota": c(np.broadcast_to(np.arange(NBLK, dtype=f32)[None, :, None], (1, NBLK, NE))),
        "headsel": c(np.broadcast_to(np.eye(NH0, dtype=f32)[:, :, None], (NH0, NH0, P))),
        "ffn_wqT": rows(x["L0_ffn_Wq"].T), "ffn_wu1T": rows(x["L0_ffn_Wu1"].T), "ffn_wu2T": c(x["L0_ffn_Wu2"].T),
        "ffn_lr": c(np.broadcast_to(x["L0_ffn_log_rel"][None, :], (P, NSLOT))),
        "gateT": rows(x["L1_ffn_gate_w"].T), "valuesT": rows(x["L0_ffn_aux_values"].T),
        "wvdT": rows(x["L0_ffn_Wvd"].T), "wvuT": c(x["L0_ffn_Wvu"].T), "wrT": c(x["L0_ffn_Wr"].T),
        "wr": c(x["L0_ffn_Wr"]), "keysT": c(x["L0_ffn_aux_keys"].T),
        "binds": c(np.stack([x["L0_attn_bv_q"], x["L0_attn_bv_k"], x["L0_attn_bv_v"]], 1)),
        "w13": c(w13.transpose(0, 2, 3, 1, 4)),
        "w2a": c(w2[:, 0:FC * P].reshape(NE, FC, P, D).transpose(0, 2, 1, 3)),
        "w2b": c(w2[:, FC * P:]),
        "wqkv": c(wqkv.transpose(2, 0, 1, 3)), "wo": rows(x["L1_attn_wo"].T),
    }


def build_program(nc, arrays, stages=6):
    aps = {n: nc.dram_tensor(f"in_{n}", a.shape, mybir.dt.from_np(a.dtype), kind="ExternalInput").ap()
           for n, a in arrays.items()}
    out = nc.dram_tensor("out_x", (T, D), F32, kind="ExternalOutput").ap()
    macaron_program(nc, aps, out, stages)


def kernel(**inputs):
    import concourse.bacc as bacc
    from concourse.bass_utils import run_bass_kernel_spmd

    nc = bacc.Bacc("TRN2", target_bir_lowering=False, num_devices=1)
    arrays = laid_out({n: np.asarray(a) for n, a in inputs.items()})
    build_program(nc, arrays)
    r = run_bass_kernel_spmd(nc, [{f"in_{n}": a for n, a in arrays.items()}], core_ids=[0])
    return np.asarray(r.results[0]["out_x"]).reshape(1, T, D)
```
